# Optimizing a Trainium2 kernel written in Bass

```python
import numpy as np
import jax
import jax.numpy as jnp

def _softmax(x, axis=-1):
    return jax.nn.softmax(x, axis=axis)

def _gelu(x):
    return jax.nn.gelu(x, approximate=True)

def _silu(x):
    return jax.nn.silu(x)

def _sigmoid(x):
    return jax.nn.sigmoid(x)

def _layernorm(x, axis=-1, eps=1e-05):
    m = jnp.mean(x, axis=axis, keepdims=True)
    v = jnp.var(x, axis=axis, keepdims=True)
    return (x - m) / jnp.sqrt(v + eps)

def _scatter_add(tgt, idx, src, axis=0):
    return tgt.at[idx].add(src)

def _segment_sum(src, seg, n):
    return jax.ops.segment_sum(src, seg, n)
kernel_name = 'mk_dlrm_tower_d1_rec_r8_4ba464'

def setup_inputs(seed: int=0):
    np.random.seed(seed)
    _w = jnp.asarray

    def _rec_inputs():
        import jax
        import jax.numpy as jnp
        _tk = jax.random.key(seed)
        ids = jnp.stack([jax.random.randint(jax.random.fold_in(_tk, 200 + f), (512,), 0, v, jnp.int32) for f, v in enumerate([125000, 1000, 1250, 1250, 1250, 1000, 1250, 1000, 1250, 1000, 12500, 12500, 1000, 12500, 1250, 1250, 12500, 12500, 1000, 1250, 12500, 1250, 12500, 12500, 1000, 1000])], axis=1)
        tbl_0 = 0.05 * jax.random.normal(jax.random.fold_in(_tk, 500 + 0), (125000, 128), jnp.float32)
        tbl_1 = 0.05 * jax.random.normal(jax.random.fold_in(_tk, 500 + 1), (1000, 128), jnp.float32)
        tbl_2 = 0.05 * jax.random.normal(jax.random.fold_in(_tk, 500 + 2), (1250, 128), jnp.float32)
        tbl_3 = 0.05 * jax.random.normal(jax.random.fold_in(_tk, 500 + 3), (1250, 128), jnp.float32)
        tbl_4 = 0.05 * jax.random.normal(jax.random.fold_in(_tk, 500 + 4), (1250, 128), jnp.float32)
        tbl_5 = 0.05 * jax.random.normal(jax.random.fold_in(_tk, 500 + 5), (1000, 128), jnp.float32)
        tbl_6 = 0.05 * jax.random.normal(jax.random.fold_in(_tk, 500 + 6), (1250, 128), jnp.float32)
        tbl_7 = 0.05 * jax.random.normal(jax.random.fold_in(_tk, 500 + 7), (1000, 128), jnp.float32)
        tbl_8 = 0.05 * jax.random.normal(jax.random.fold_in(_tk, 500 + 8), (1250, 128), jnp.float32)
        tbl_9 = 0.05 * jax.random.normal(jax.random.fold_in(_tk, 500 + 9), (1000, 128), jnp.float32)
        tbl_10 = 0.05 * jax.random.normal(jax.random.fold_in(_tk, 500 + 10), (12500, 128), jnp.float32)
        tbl_11 = 0.05 * jax.random.normal(jax.random.fold_in(_tk, 500 + 11), (12500, 128), jnp.float32)
        tbl_12 = 0.05 * jax.random.normal(jax.random.fold_in(_tk, 500 + 12), (1000, 128), jnp.float32)
        tbl_13 = 0.05 * jax.random.normal(jax.random.fold_in(_tk, 500 + 13), (12500, 128), jnp.float32)
        tbl_14 = 0.05 * jax.random.normal(jax.random.fold_in(_tk, 500 + 14), (1250, 128), jnp.float32)
        tbl_15 = 0.05 * jax.random.normal(jax.random.fold_in(_tk, 500 + 15), (1250, 128), jnp.float32)
        tbl_16 = 0.05 * jax.random.normal(jax.random.fold_in(_tk, 500 + 16), (12500, 128), jnp.float32)
        tbl_17 = 0.05 * jax.random.normal(jax.random.fold_in(_tk, 500 + 17), (12500, 128), jnp.float32)
        tbl_18 = 0.05 * jax.random.normal(jax.random.fold_in(_tk, 500 + 18), (1000, 128), jnp.float32)
        tbl_19 = 0.05 * jax.random.normal(jax.random.fold_in(_tk, 500 + 19), (1250, 128), jnp.float32)
        tbl_20 = 0.05 * jax.random.normal(jax.random.fold_in(_tk, 500 + 20), (12500, 128), jnp.float32)
        tbl_21 = 0.05 * jax.random.normal(jax.random.fold_in(_tk, 500 + 21), (1250, 128), jnp.float32)
        tbl_22 = 0.05 * jax.random.normal(jax.random.fold_in(_tk, 500 + 22), (12500, 128), jnp.float32)
        tbl_23 = 0.05 * jax.random.normal(jax.random.fold_in(_tk, 500 + 23), (12500, 128), jnp.float32)
        tbl_24 = 0.05 * jax.random.normal(jax.random.fold_in(_tk, 500 + 24), (1000, 128), jnp.float32)
        tbl_25 = 0.05 * jax.random.normal(jax.random.fold_in(_tk, 500 + 25), (1000, 128), jnp.float32)
        _rk = jax.random.fold_in(_tk, 7)
        r_dense_x = -0.000514642 + 1.00011 * jax.random.normal(jax.random.fold_in(_rk, 101), (512, 128), jnp.float32)
        W_top1 = 0.0456912 * jax.random.normal(jax.random.fold_in(_tk, 801), (479, 512), jnp.float32)
        W_top2 = 0.0441942 * jax.random.normal(jax.random.fold_in(_tk, 802), (512, 256), jnp.float32)
        W_top3 = 0.0625 * jax.random.normal(jax.random.fold_in(_tk, 803), (256, 1), jnp.float32)
        b_top1 = jnp.zeros((512,), jnp.float32)
        b_top2 = jnp.zeros((256,), jnp.float32)
        return (r_dense_x, ids, tbl_0, tbl_1, tbl_2, tbl_3, tbl_4, tbl_5, tbl_6, tbl_7, tbl_8, tbl_9, tbl_10, tbl_11, tbl_12, tbl_13, tbl_14, tbl_15, tbl_16, tbl_17, tbl_18, tbl_19, tbl_20, tbl_21, tbl_22, tbl_23, tbl_24, tbl_25, W_top1, b_top1, W_top2, b_top2, W_top3)
    r_dense_x, ids, tbl_0, tbl_1, tbl_2, tbl_3, tbl_4, tbl_5, tbl_6, tbl_7, tbl_8, tbl_9, tbl_10, tbl_11, tbl_12, tbl_13, tbl_14, tbl_15, tbl_16, tbl_17, tbl_18, tbl_19, tbl_20, tbl_21, tbl_22, tbl_23, tbl_24, tbl_25, W_top1, b_top1, W_top2, b_top2, W_top3 = _rec_inputs()

    def _L0_rec_setup():
        import jax, jax.numpy as jnp
        import numpy as np
        F = 26
        D = 128
        B = 2048
        _TRIU_I, _TRIU_J = np.triu_indices(F + 1, k=1)
        _TRIU_I = jnp.asarray(_TRIU_I)
        _TRIU_J = jnp.asarray(_TRIU_J)
        key = jax.random.key(seed)
        k1, k2 = jax.random.split(key)
        sparse_x = jax.random.normal(k1, (B, F, D), dtype=jnp.float32)
        dense_x = jax.random.normal(k2, (B, D), dtype=jnp.float32)
        return {'sparse_x': sparse_x, 'dense_x': dense_x}
    _L0_rec_all = _L0_rec_setup()
    _L0_rec_in = {k: v for k, v in _L0_rec_all.items() if k in ()}
    del _L0_rec_all
    return {'r_dense_x': r_dense_x, 'ids': ids, 'tbl_0': tbl_0, 'tbl_1': tbl_1, 'tbl_2': tbl_2, 'tbl_3': tbl_3, 'tbl_4': tbl_4, 'tbl_5': tbl_5, 'tbl_6': tbl_6, 'tbl_7': tbl_7, 'tbl_8': tbl_8, 'tbl_9': tbl_9, 'tbl_10': tbl_10, 'tbl_11': tbl_11, 'tbl_12': tbl_12, 'tbl_13': tbl_13, 'tbl_14': tbl_14, 'tbl_15': tbl_15, 'tbl_16': tbl_16, 'tbl_17': tbl_17, 'tbl_18': tbl_18, 'tbl_19': tbl_19, 'tbl_20': tbl_20, 'tbl_21': tbl_21, 'tbl_22': tbl_22, 'tbl_23': tbl_23, 'tbl_24': tbl_24, 'tbl_25': tbl_25, 'W_top1': W_top1, 'b_top1': b_top1, 'W_top2': W_top2, 'b_top2': b_top2, 'W_top3': W_top3}

def reference(r_dense_x, ids, tbl_0, tbl_1, tbl_2, tbl_3, tbl_4, tbl_5, tbl_6, tbl_7, tbl_8, tbl_9, tbl_10, tbl_11, tbl_12, tbl_13, tbl_14, tbl_15, tbl_16, tbl_17, tbl_18, tbl_19, tbl_20, tbl_21, tbl_22, tbl_23, tbl_24, tbl_25, W_top1, b_top1, W_top2, b_top2, W_top3):
    import jax
    import jax.numpy as jnp

    def _L0_rec_ref(sparse_x, dense_x):
        import jax, jax.numpy as jnp
        import numpy as np
        F = 26
        D = 128
        B = 2048
        _TRIU_I, _TRIU_J = np.triu_indices(F + 1, k=1)
        _TRIU_I = jnp.asarray(_TRIU_I)
        _TRIU_J = jnp.asarray(_TRIU_J)
        combined = jnp.concatenate([sparse_x, dense_x[:, None, :]], axis=1)
        interact = jnp.einsum('bfd,bgd->bfg', combined, combined)
        return interact[:, _TRIU_I, _TRIU_J]
    e = jnp.stack([tbl_0[ids[:, 0]], tbl_1[ids[:, 1]], tbl_2[ids[:, 2]], tbl_3[ids[:, 3]], tbl_4[ids[:, 4]], tbl_5[ids[:, 5]], tbl_6[ids[:, 6]], tbl_7[ids[:, 7]], tbl_8[ids[:, 8]], tbl_9[ids[:, 9]], tbl_10[ids[:, 10]], tbl_11[ids[:, 11]], tbl_12[ids[:, 12]], tbl_13[ids[:, 13]], tbl_14[ids[:, 14]], tbl_15[ids[:, 15]], tbl_16[ids[:, 16]], tbl_17[ids[:, 17]], tbl_18[ids[:, 18]], tbl_19[ids[:, 19]], tbl_20[ids[:, 20]], tbl_21[ids[:, 21]], tbl_22[ids[:, 22]], tbl_23[ids[:, 23]], tbl_24[ids[:, 24]], tbl_25[ids[:, 25]]], axis=1)
    z = _L0_rec_ref(e, r_dense_x)
    z = z.reshape(z.shape[0], -1)
    h = jnp.concatenate([z, r_dense_x], axis=1)
    h = jnp.maximum(h @ W_top1 + b_top1, 0.0)
    h = jnp.maximum(h @ W_top2 + b_top2, 0.0)
    y = h @ W_top3
    return y

_drawn_inputs = setup_inputs


def setup_inputs(seed=0):
    import zlib

    import numpy as np

    out = dict(_drawn_inputs(seed))
    spreads = {'b_top1': (0.0, 0.1), 'b_top2': (0.0, 0.1)}
    factors = {}
    for name, (base, spread) in spreads.items():
        noise = np.random.default_rng([zlib.crc32(name.encode()), seed]).standard_normal(out[name].shape)
        drawn = base * np.exp(spread * noise) if base else spread * noise
        out[name] = jnp.asarray(drawn.astype(out[name].dtype))
    for name, factor in factors.items():
        out[name] = (out[name] * factor).astype(out[name].dtype)
    return out
```

```python
from contextlib import ExitStack

import concourse.bass as bass
from concourse import mybir

F32 = mybir.dt.float32
F16 = mybir.dt.float16
BF16 = mybir.dt.bfloat16
U32 = mybir.dt.uint32
I32 = mybir.dt.int32
ALU = mybir.AluOpType
ACT = mybir.ActivationFunctionType

P = 128
BATCH = 512
D = 128
TILES = BATCH // P
NTAB = 26
NVEC = NTAB + 1
SLOTS = 32
PART_COLS = 7
QUAD = 4
NCOL = NVEC - 1
HALF = 64
H1, H2 = 512, 256
HC1, HC2 = H1 // P, H2 // P
BANK = 512

HOT = [1, 5, 7, 9, 12, 18, 24]
HOT_PARTS = 125
COLD = [f for f in range(NTAB) if f not in HOT]
GROUP = 4
SLOT_FIELD = [NTAB] + COLD + HOT
TURNED = 1 + len(COLD)
GROUPS = [list(range(a, min(a + GROUP, TURNED))) for a in range(0, TURNED, GROUP)]
NG = len(GROUPS)
PART_RANGE = [(1 + PART_COLS * s, min(NVEC, 1 + PART_COLS * (s + 1))) for s in range(4)]


def build(nc, x, ids, ids_t, tables, w1_pairs, w1_dense, b1, w2, b2, w3, out):
    hot_rows = [tables[f].shape[0] // HOT_PARTS for f in HOT]
    max_chunks = max(hot_rows)
    n_hot = len(HOT)

    with ExitStack() as ctx:
        def sb(name, shape, dt):
            return ctx.enter_context(nc.sbuf_tensor(name, shape, dt))

        def psum(name, shape, dt=F32):
            return ctx.enter_context(nc.psum_tensor(name, shape, dt))

        def sem(name):
            return ctx.enter_context(nc.semaphore(name))

        idx = sb("idx", [P, TILES, NTAB], U32)
        rows = sb("rows", [P, TILES, TURNED, D], F32)
        ident = sb("ident", [P, P], F32)
        XT = sb("XT", [P, BATCH, SLOTS], F32)
        denseT = sb("denseT", [P, BATCH], F32)
        PAIRS = sb("PAIRS", [P, PART_COLS, BATCH], F32)
        W1P = sb("W1P", [P, PART_COLS, H1], F32)
        W1D = sb("W1D", [P, H1], F32)
        W2 = sb("W2", [P, HC1, H2], F32)
        W3 = sb("W3", [P, HC2], F32)
        B1 = sb("B1", [P, HC1], F32)
        B2 = sb("B2", [P, HC2], F32)
        h1 = sb("h1", [P, 2, HC1, P], F32)
        h2 = sb("h2", [P, 2, HC2, P], F32)
        y = sb("y", [1, BATCH], F32)
        hot_tab = [sb(f"hot_tab{i}", [P, max_chunks * D], F32) for i in range(2)]
        hot_rest = [sb(f"hot_rest{i}", [P, max_chunks * D], F32) for i in range(2)]
        hot_low = [sb(f"hot_low{i}", [P, max_chunks * D], BF16) for i in range(2)]
        hot_ids = [sb(f"hot_ids{i}", [P, BATCH], I32) for i in range(2)]
        hot_idsf = sb("hot_idsf", [P, BATCH], F16)
        onehot = [sb(f"onehot{i}", [P, max_chunks, BATCH], BF16) for i in range(2)]
        row_no_i = {n: sb(f"row_no_i{n}", [P, n], I32) for n in sorted(set(hot_rows))}
        row_no = {n: sb(f"row_no{n}", [P, n], F32) for n in sorted(set(hot_rows))}

        turn_ps = [psum(f"turn_ps{i}", [P, BANK]) for i in range(2)]
        gram_ps = psum("gram_ps", [P, 4, BANK])
        h1_ps = psum("h1_ps", [P, HC1, P])
        h2_ps = psum("h2_ps", [P, BANK])

        idx_in = sem("idx_in")
        dense_in = sem("dense_in")
        w1_in = sem("w1_in")
        w2_in = sem("w2_in")
        bias_in = sem("bias_in")
        hot_in = [sem(f"hot_in{i}") for i in range(2)]
        gathered = [sem(f"gathered{g}") for g in range(NG)]
        ident_zero = sem("ident_zero")
        ident_ready = sem("ident_ready")
        iota_ready = sem("iota_ready")
        row_no_ready = sem("row_no_ready")
        cleared = sem("cleared")
        rest_ready = sem("rest_ready")
        low_ready = sem("low_ready")
        idsf_ready = sem("idsf_ready")
        onehot_ready = sem("onehot_ready")
        turned = sem("turned")
        turn_read = {"act": sem("turn_read_act"), "dve": sem("turn_read_dve")}
        gram_ready = sem("gram_ready")
        pairs_act = sem("pairs_act")
        pairs_dve = sem("pairs_dve")
        h1_sum = sem("h1_sum")
        h1_ready = sem("h1_ready")
        h2_sum = sem("h2_sum")
        h2_ready = sem("h2_ready")
        y_sum = sem("y_sum")
        y_ready = sem("y_ready")
        stored = sem("stored")
        block = ctx.enter_context(nc.Block())

        early = [("turn", 0, g) for g in range(NG)] + [("turn", 1, g) for g in range(NG)]
        fills = []
        for n in range(n_hot):
            fills.append(("hot", n))
            if n >= 1 and n - 1 < len(early):
                fills.append(early[n - 1])
        done_early = max(0, n_hot - 1)
        before_gram = [[] for _ in range(TILES)]
        before_gram[0] = early[done_early:NG]
        next_tile = [[] for _ in range(TILES)]
        next_tile[0] = early[max(done_early, NG):]
        for t in range(1, TILES - 1):
            next_tile[t] = [("turn", t + 1, g) for g in range(NG)]
        fills += before_gram[0]
        for t in range(TILES):
            fills += next_tile[t]
        fill_no = {item: i for i, item in enumerate(fills)}
        n_first = len(fills) - sum(len(later) for later in next_tile)
        reader = ["act"] * n_first + ["dve"] * (len(fills) - n_first)

        def wait_emptied(eng, upto):
            for who in ("act", "dve"):
                count = reader[:upto + 1].count(who)
                if count:
                    eng.wait_ge(turn_read[who], count)

        def fills_for_tile(t):
            return max(fill_no[i] for i in [("hot", n) for n in range(n_hot)] + [("turn", t, g) for g in range(NG)])

        def gather_count(g):
            return sum(1 for s in GROUPS[g] if s > 0)

        @block.sync
        def _(sp):
            sp.dma_start(idx[:], ids.bitcast(U32).rearrange("(t p) f -> p t f", p=P)).then_inc(idx_in, 16)

            def load_hot(n):
                if n >= 2:
                    sp.wait_ge(turned, fill_no[("hot", n - 2)] + 1)
                f, c = HOT[n], hot_rows[n]
                sp.dma_start(hot_tab[n % 2][0:HOT_PARTS, 0:c * D],
                             tables[f].rearrange("(p c) d -> p (c d)", c=c)).then_inc(hot_in[n % 2], 16)
                sp.dma_start(hot_ids[n % 2][:], ids_t[f:f + 1, :].broadcast_to([P, BATCH])).then_inc(hot_in[n % 2], 16)

            load_hot(0)
            load_hot(1)
            sp.dma_start(rows[:, :, 0, :], x.rearrange("(t p) d -> p t d", p=P)).then_inc(dense_in, 16)
            load_hot(2)
            sp.dma_start(W1P[:], w1_pairs).then_inc(w1_in, 16)
            sp.dma_start(W1D[:], w1_dense).then_inc(w1_in, 16)
            sp.dma_start(W2[:], w2.rearrange("(c p) n -> p c n", p=P)).then_inc(w2_in, 16)
            with nc.allow_non_contiguous_dma(reason="a few hundred words of biases and W_top3"):
                sp.dma_start(W3[:], w3.rearrange("(c p) n -> p (c n)", p=P)).then_inc(w2_in, 16)
                sp.dma_start(B1[:], b1.rearrange("(c p) -> p c", p=P)).then_inc(bias_in, 16)
                sp.dma_start(B2[:], b2.rearrange("(c p) -> p c", p=P)).then_inc(bias_in, 16)
            for n in range(3, n_hot):
                load_hot(n)
            sp.wait_ge(y_ready, TILES)
            sp.dma_start(out.rearrange("b o -> o b"), y[:]).then_inc(stored, 16)
            sp.wait_ge(stored, 16)

        @block.gpsimd
        def _(pool):
            pool.wait_ge(ident_zero, 1)
            pool.affine_select(out=ident[:], in_=ident[:], compare_op=ALU.not_equal, fill=1.0, base=0,
                               pattern=[[-1, P]], channel_multiplier=1).then_inc(ident_ready, 1)
            for n in sorted(row_no_i):
                pool.iota(row_no_i[n][:], pattern=[[1, n]], base=0, channel_multiplier=n).then_inc(iota_ready, 1)
            pool.wait_ge(idx_in, 16)
            for t in range(TILES):
                for g in range(NG):
                    if t:
                        pool.wait_ge(gathered[g], 16 * gather_count(g) * t)
                    for s in GROUPS[g]:
                        if s:
                            f = SLOT_FIELD[s]
                            pool.indirect_dma_start(
                                rows[:, t, s, :], None, tables[f],
                                bass.IndirectOffsetOnAxis(ap=idx[:, t, f:f + 1], axis=0)).then_inc(gathered[g], 16)

        def empty_bank(eng, copy, i):
            eng.wait_ge(turned, i + 1)
            ps = turn_ps[i % 2]
            item = fills[i]
            if item[0] == "hot":
                copy(XT[:, :, TURNED + item[1]], ps[:]).then_inc(turn_read[reader[i]], 1)
                return
            _, t, g = item
            s0, n = GROUPS[g][0], len(GROUPS[g])
            here = slice(t * P, (t + 1) * P)
            if s0 == 0:
                copy(denseT[:, here], ps[:, 0:P])
            copy(XT[:, here, s0:s0 + n].rearrange("d s f -> d f s"),
                 ps[:, 0:n * P].rearrange("d (f s) -> d f s", f=n)).then_inc(turn_read[reader[i]], 1)

        def move_pairs(eng, copy, t, half, quads, done):
            eng.wait_ge(gram_ready, 2 * t + half + 1)
            for j in quads:
                for s in range(4):
                    lo, hi = PART_RANGE[s]
                    src = gram_ps[32 * j:32 * j + 32, :, 0:QUAD * QUAD * NCOL] \
                        .rearrange("a k (q n) -> a k q n", q=QUAD)[:, :, :, j * NCOL + lo - 1:j * NCOL + hi - 1]
                    b0 = t * P + half * HALF
                    dst = PAIRS[32 * s:32 * s + 32, 0:hi - lo, b0:b0 + HALF] \
                        .rearrange("a n (k q j) -> a k q j n", q=QUAD, j=QUAD)[:, :, :, j, :]
                    last = copy(dst, src)
            last.then_inc(done, 1)

        @block.scalar
        def _(act):
            def copy(dst, src):
                return nc.scalar.copy(dst, src)

            def relu1(t, n):
                act.wait_ge(h1_sum, t + 1)
                nc.scalar.activation(h1[:, t % 2, n, :], h1_ps[:, n, :], ACT.Relu,
                                     bias=B1[:, n:n + 1]).then_inc(h1_ready, 1)

            def relu2(t):
                for n in range(HC2):
                    act.wait_ge(h2_sum, t + 1)
                    nc.scalar.activation(h2[:, t % 2, n, :], h2_ps[:, n * P:(n + 1) * P], ACT.Relu,
                                         bias=B2[:, n:n + 1]).then_inc(h2_ready, 1)
                act.wait_ge(y_sum, t + 1)
                copy(y[0:1, t * P:(t + 1) * P], h2_ps[0:1, H2:H2 + P]).then_inc(y_ready, 1)

            for i in range(n_first):
                empty_bank(act, copy, i)
            act.wait_ge(bias_in, 32)
            for t in range(TILES):
                move_pairs(act, copy, t, 0, (0, 1), pairs_act)
                if t:
                    for n in range(HC1):
                        relu1(t - 1, n)
                move_pairs(act, copy, t, 1, (0, 1), pairs_act)
                if t:
                    relu2(t - 1)
            for n in range(HC1):
                relu1(TILES - 1, n)
            relu2(TILES - 1)

        @block.vector
        def _(dve):
            def copy(dst, src):
                return nc.vector.tensor_copy(dst, src)

            nc.vector.memset(ident[:], 0.0).then_inc(ident_zero, 1)
            nc.vector.memset(XT[:, :, NVEC:SLOTS], 0.0).then_inc(cleared, 1)
            lo, hi = PART_RANGE[3]
            nc.vector.memset(PAIRS[96:128, hi - lo:PART_COLS, :], 0.0).then_inc(cleared, 1)
            for k, n in enumerate(sorted(row_no_i)):
                dve.wait_ge(iota_ready, k + 1)
                copy(row_no[n][:], row_no_i[n][:]).then_inc(row_no_ready, 1)
            dve.wait_ge(row_no_ready, len(row_no))
            for n in range(n_hot):
                b, c = n % 2, hot_rows[n]
                part = slice(0, HOT_PARTS)
                dve.wait_ge(hot_in[b], 32 * (n // 2 + 1))
                if n >= 2:
                    dve.wait_ge(turned, fill_no[("hot", n - 2)] + 1)
                if n >= 1:
                    dve.wait_ge(onehot_ready, sum(hot_rows[:n]))
                copy(hot_idsf[:], hot_ids[b][:]).then_inc(idsf_ready, 1)
                high = hot_tab[b][part, 0:c * D].bitcast(BF16)[:, 1::2]
                nc.vector.tensor_tensor(hot_rest[b][part, 0:c * D], hot_tab[b][part, 0:c * D], high,
                                        ALU.subtract).then_inc(rest_ready, 1)
                dve.wait_ge(idsf_ready, n + 1)
                for k in range(c):
                    nc.vector.tensor_scalar(onehot[b][part, k, :], hot_idsf[part, :], row_no[c][part, k:k + 1], None,
                                            ALU.is_equal).then_inc(onehot_ready, 1)
                dve.wait_ge(rest_ready, n + 1)
                mid = hot_rest[b][part, 0:c * D].bitcast(BF16)[:, 1::2]
                nc.vector.tensor_tensor(hot_low[b][part, 0:c * D], hot_rest[b][part, 0:c * D], mid,
                                        ALU.subtract).then_inc(low_ready, 1)
            for t in range(TILES):
                move_pairs(dve, copy, t, 0, (2, 3), pairs_dve)
                if t == 0:
                    for item in next_tile[0]:
                        empty_bank(dve, copy, fill_no[item])
                move_pairs(dve, copy, t, 1, (2, 3), pairs_dve)
                if t:
                    for item in next_tile[t]:
                        empty_bank(dve, copy, fill_no[item])

        @block.tensor
        def _(pe):
            pe.wait_ge(ident_ready, 1)

            def bank_free(i):
                if i >= 2:
                    wait_emptied(pe, i - 2)

            def fill(item):
                i = fill_no[item]
                ps = turn_ps[i % 2]
                bank_free(i)
                if item[0] == "hot":
                    n = item[1]
                    b, c = n % 2, hot_rows[n]
                    part = slice(0, HOT_PARTS)
                    words = [hot_tab[b][part, 0:c * D].bitcast(BF16), hot_rest[b][part, 0:c * D].bitcast(BF16)]
                    pe.wait_ge(rest_ready, n + 1)
                    for which in range(3):
                        if which == 2:
                            pe.wait_ge(low_ready, n + 1)
                        for k in range(c):
                            if which == 0:
                                pe.wait_ge(onehot_ready, sum(hot_rows[:n]) + k + 1)
                            if which < 2:
                                w = words[which][:, 2 * k * D + 1:2 * (k + 1) * D:2]
                            else:
                                w = hot_low[b][part, k * D:(k + 1) * D]
                            last = nc.tensor.matmul(ps[:], w, onehot[b][part, k, :],
                                                    start=(which == 0 and k == 0), stop=(which == 2 and k == c - 1))
                    last.then_inc(turned, 1)
                    return
                _, t, g = item
                if gather_count(g):
                    pe.wait_ge(gathered[g], 16 * gather_count(g) * (t + 1))
                if GROUPS[g][0] == 0:
                    pe.wait_ge(dense_in, 16)
                for k, s in enumerate(GROUPS[g]):
                    last = nc.tensor.transpose(ps[:, k * P:(k + 1) * P], rows[:, t, s, :], ident[:])
                last.then_inc(turned, 1)

            def gram(t, half):
                wait_emptied(pe, fills_for_tile(t))
                b = 2 * t + half
                if b:
                    pe.wait_ge(pairs_act, b)
                    pe.wait_ge(pairs_dve, b)
                for q in range(HALF // QUAD):
                    s0 = t * P + half * HALF + q * QUAD
                    four = XT[:, s0:s0 + QUAD, :]
                    o = (q % QUAD) * QUAD * NCOL
                    last = nc.tensor.matmul(gram_ps[:, q // QUAD, o:o + QUAD * NCOL],
                                            four.rearrange("d s f -> d (s f)"), four[:, :, 1:NVEC],
                                            start=True, stop=True)
                last.then_inc(gram_ready, 1)

            def layer1(t, s0, ns, final):
                here = slice(t * P + s0, t * P + s0 + ns)
                if t and s0 == 0:
                    pe.wait_ge(h1_ready, HC1 * t)
                for n in range(HC1):
                    hid = slice(n * P, (n + 1) * P)
                    o = h1_ps[:, n, s0:s0 + ns]
                    nc.tensor.matmul(o, W1D[:, hid], denseT[:, here], start=True, stop=False)
                    for k in range(PART_COLS):
                        last = nc.tensor.matmul(o, W1P[:, k, hid], PAIRS[:, k, here], start=False,
                                                stop=(k == PART_COLS - 1))
                if final:
                    last.then_inc(h1_sum, 1)

            def layer23(t):
                if t:
                    pe.wait_ge(y_ready, t)
                for n in range(HC2):
                    for k in range(HC1):
                        if n == 0:
                            pe.wait_ge(h1_ready, HC1 * t + k + 1)
                        last = nc.tensor.matmul(h2_ps[:, n * P:(n + 1) * P], W2[:, k, n * P:(n + 1) * P],
                                                h1[:, t % 2, k, :], start=(k == 0), stop=(k == HC1 - 1))
                last.then_inc(h2_sum, 1)
                pe.wait_ge(h2_ready, HC2 * (t + 1))
                for k in range(HC2):
                    last = nc.tensor.matmul(h2_ps[0:1, H2:H2 + P], W3[:, k:k + 1], h2[:, t % 2, k, :],
                                            start=(k == 0), stop=(k == HC2 - 1))
                last.then_inc(y_sum, 1)

            for item in fills[:n_first]:
                fill(item)
            pe.wait_ge(cleared, 2)
            pe.wait_ge(w1_in, 32)
            pe.wait_ge(w2_in, 32)
            for t in range(TILES):
                gram(t, 0)
                if t:
                    pe.wait_ge(pairs_act, 2 * t)
                    layer1(t - 1, 0, P, True)
                else:
                    for item in next_tile[0]:
                        fill(item)
                gram(t, 1)
                if t:
                    for item in next_tile[t]:
                        fill(item)
                    layer23(t - 1)
            t = TILES - 1
            pe.wait_ge(pairs_act, 2 * t + 1)
            pe.wait_ge(pairs_dve, 2 * t + 1)
            layer1(t, 0, HALF, False)
            pe.wait_ge(pairs_act, 2 * t + 2)
            pe.wait_ge(pairs_dve, 2 * t + 2)
            layer1(t, HALF, HALF, True)
            layer23(t)


def pair_rows():
    rows = []
    slot = {f: s for s, f in enumerate(SLOT_FIELD)}
    n = 0
    for i in range(NVEC):
        for j in range(i + 1, NVEC):
            a, g = sorted((slot[i], slot[j]))
            s, k = divmod(g - 1, PART_COLS)
            rows.append((32 * s + a, k, n))
            n += 1
    return rows, n


def kernel(**inputs):
    import numpy as _np
    import concourse.bacc as _bacc
    from concourse import mybir as _mybir
    from concourse.bass_utils import run_bass_kernel_spmd as _run

    nc = _bacc.Bacc("TRN2", target_bir_lowering=False, num_devices=1)
    arrays, args = {}, {}

    def give(name, a):
        a = _np.ascontiguousarray(a)
        arrays[f"in_{name}_dram"] = a
        args[name] = nc.dram_tensor(f"in_{name}_dram", a.shape, _mybir.dt.from_np(a.dtype), kind="ExternalInput").ap()
        return args[name]

    x = give("r_dense_x", inputs["r_dense_x"])
    ids = give("ids", inputs["ids"])
    ids_t = give("ids_t", _np.asarray(inputs["ids"]).T)
    tables = [give(f"tbl_{f}", inputs[f"tbl_{f}"]) for f in range(NTAB)]
    w1 = _np.asarray(inputs["W_top1"])
    where, n_pairs = pair_rows()
    p, k, r = (_np.array(c) for c in zip(*where))
    w1_pairs = _np.zeros((P, PART_COLS, H1), w1.dtype)
    w1_pairs[p, k] = w1[r]
    w1p = give("w1_pairs", w1_pairs)
    w1d = give("w1_dense", w1[n_pairs:])
    b1 = give("b_top1", inputs["b_top1"])
    w2 = give("W_top2", inputs["W_top2"])
    b2 = give("b_top2", inputs["b_top2"])
    w3 = give("W_top3", inputs["W_top3"])
    out = nc.dram_tensor("out_0_dram", (BATCH, 1), _mybir.dt.float32, kind="ExternalOutput").ap()
    build(nc, x, ids, ids_t, tables, w1p, w1d, b1, w2, b2, w3, out)
    r = _run(nc, [arrays], core_ids=[0])
    return r.results[0]["out_0_dram"]
```

```python
from contextlib import ExitStack

import concourse.bass as bass
from concourse import mybir

F32 = mybir.dt.float32
F16 = mybir.dt.float16
BF16 = mybir.dt.bfloat16
U32 = mybir.dt.uint32
I32 = mybir.dt.int32
ALU = mybir.AluOpType
ACT = mybir.ActivationFunctionType

P = 128
BATCH = 512
D = 128
TILES = BATCH // P
NTAB = 26
NVEC = NTAB + 1
SLOTS = 32
FIRST = 3
FEW = [(0, 1), (0, 2), (1, 2)]
QUAD = 4
NCOL = NVEC - FIRST
PART_COLS = NCOL // 4
BATCHES = 4
BSAMP = P // BATCHES
H1, H2 = 512, 256
HC1, HC2 = H1 // P, H2 // P
BANK = 512
WARM_UP = 9
PER_TILE = 2
LATE = 2
RING = 3

HOT = [1, 5, 7, 9, 12]
HOT_ROWS = 1000
HOT_PARTS = 125
CHUNKS = HOT_ROWS // HOT_PARTS
COLD = [f for f in range(NTAB) if f not in HOT]
GROUP = 4
SLOT_FIELD = [NTAB] + COLD + HOT
TURNED = 1 + len(COLD)
GROUPS = [list(range(a, min(a + GROUP, TURNED))) for a in range(0, TURNED, GROUP)]
NG = len(GROUPS)


def build(nc, x, ids, ids_t, chunk_numbers, tables, w1_pairs, w1_dense, b1, w2, b2, w3, out):
    n_hot = len(HOT)
    assert all(tables[f].shape[0] == HOT_ROWS for f in HOT)

    with ExitStack() as ctx:
        def sb(name, shape, dt):
            return ctx.enter_context(nc.sbuf_tensor(name, shape, dt))

        def psum(name, shape, dt=F32):
            return ctx.enter_context(nc.psum_tensor(name, shape, dt))

        def sem(name):
            return ctx.enter_context(nc.semaphore(name))

        idx = sb("idx", [P, TILES, NTAB], U32)
        rows = sb("rows", [P, TILES, TURNED, D], F32)
        ident = sb("ident", [P, P], F32)
        XT = sb("XT", [P, BATCH, SLOTS], F32)
        denseT = sb("denseT", [P, BATCH], F32)
        few = sb("few", [P, TILES, SLOTS], F32)
        few_prod = sb("few_prod", [P, D], F32)
        fewT = sb("fewT", [SLOTS, BATCH], F32)
        PAIRS = sb("PAIRS", [P, PART_COLS, BATCH], F32)
        W1P = sb("W1P", [P, PART_COLS, H1], F32)
        W1D = sb("W1D", [P, H1], F32)
        W2 = sb("W2", [P, HC1, H2], F32)
        W3 = sb("W3", [P, HC2], F32)
        B1 = sb("B1", [P, HC1], F32)
        B2 = sb("B2", [P, HC2], F32)
        h1 = sb("h1", [P, HC1, P], F32)
        h2 = sb("h2", [P, HC2, P], F32)
        y = sb("y", [1, BATCH], F32)
        hot_tab = [sb(f"hot_tab{i}", [P, CHUNKS * D], F32) for i in range(RING)]
        hot_rest = [sb(f"hot_rest{i}", [P, CHUNKS * D], F32) for i in range(2)]
        hot_low = [sb(f"hot_low{i}", [P, CHUNKS * D], BF16) for i in range(2)]
        hot_ids = [sb(f"hot_ids{i}", [P, BATCH], I32) for i in range(RING)]
        hot_chunk = [sb(f"hot_chunk{i}", [P, BATCH], F16) for i in range(2)]
        chunk_no = sb("chunk_no", [P, CHUNKS, BATCH], F16)
        onehot = [sb(f"onehot{i}", [P, CHUNKS, BATCH], BF16) for i in range(2)]
        first_row_i = sb("first_row_i", [P, 1], I32)
        first_row = sb("first_row", [P, 1], F32)

        turn_ps = [psum(f"turn_ps{i}", [P, BANK]) for i in range(2)]
        gram_ps = psum("gram_ps", [P, 4, BANK])
        h1_ps = psum("h1_ps", [P, HC1, P])
        h2_ps = psum("h2_ps", [P, BANK])

        idx_in = sem("idx_in")
        dense_in = sem("dense_in")
        w1_in = sem("w1_in")
        w2_in = sem("w2_in")
        bias_in = sem("bias_in")
        hot_in = [sem(f"hot_in{i}") for i in range(RING)]
        ids_in = [sem(f"ids_in{i}") for i in range(RING)]
        gathered = [sem(f"gathered{g}") for g in range(NG)]
        ident_zero = sem("ident_zero")
        ident_ready = sem("ident_ready")
        iota_ready = sem("iota_ready")
        first_row_ready = sem("first_row_ready")
        chunk_no_in = sem("chunk_no_in")
        cleared = sem("cleared")
        rest_ready = sem("rest_ready")
        low_ready = sem("low_ready")
        chunk_ready = sem("chunk_ready")
        onehot_ready = sem("onehot_ready")
        turned = sem("turned")
        turn_read = {"act": sem("turn_read_act"), "dve": sem("turn_read_dve")}
        gram_ready = sem("gram_ready")
        few_step = sem("few_step")
        pairs_full = sem("pairs_full")
        pairs_act = sem("pairs_act")
        pairs_dve = sem("pairs_dve")
        h1_sum = sem("h1_sum")
        h1_ready = sem("h1_ready")
        h2_sum = sem("h2_sum")
        h2_ready = sem("h2_ready")
        h1_ready_dve = sem("h1_ready_dve")
        h2_ready_dve = sem("h2_ready_dve")
        y_sum = sem("y_sum")
        y_ready = sem("y_ready")
        stored = sem("stored")
        block = ctx.enter_context(nc.Block())

        whole, by_tile = range(n_hot - PER_TILE), range(n_hot - PER_TILE, n_hot)
        fills, early = [], [("turn", 0, g) for g in range(NG)]
        for n in whole:
            fills.append(("hot", n, 0, TILES))
            if n:
                fills.append(early.pop(0))
        for n in by_tile:
            fills += [early.pop(0), ("hot", n, 0, 1)]
        fills += early
        n_first = len(fills)
        between = [[] for _ in range(TILES)]
        late = [[] for _ in range(TILES)]
        for t in range(TILES - 1):
            turns = [("turn", t + 1, g) for g in range(NG)]
            hots = [("hot", n, t + 1, t + 2) for n in by_tile]
            between[t] = hots[:1] + turns[:-LATE]
            late[t] = hots[1:] + turns[-LATE:]
        for t in range(TILES):
            fills += between[t] + late[t]
        fill_no = {item: i for i, item in enumerate(fills)}
        shared = between[0] + sum(late, [])
        reader = ["act" if i < n_first or item in shared[1::2] else "dve" for i, item in enumerate(fills)]

        def fill_bank(i):
            early = [turn_ps[0][:], turn_ps[1][:], gram_ps[:, 0, :], gram_ps[:, 1, :]]
            return early[i % 4] if i < n_first else turn_ps[i % 2][:]

        def bank_before(i):
            if i < n_first:
                return i - 4
            return max([j for j in range(n_first) if j % 4 == i % 2], default=-1) if i - 2 < n_first else i - 2

        def wait_emptied(eng, upto):
            for who in ("act", "dve"):
                count = reader[:upto + 1].count(who)
                if count:
                    eng.wait_ge(turn_read[who], count)

        def fills_for_tile(t):
            return max(i for i, item in enumerate(fills)
                       if (item[2] <= t < item[3] if item[0] == "hot" else item[1] == t))

        def hot_done(n):
            return max(i for i, item in enumerate(fills) if item[:2] == ("hot", n)) + 1

        def gather_count(g):
            return sum(1 for s in GROUPS[g] if s > 0)

        @block.sync
        def _(sp):
            def load_hot(n):
                if n >= RING:
                    sp.wait_ge(turned, hot_done(n - RING))
                f = HOT[n]
                if n == 0:
                    sp.dma_start(idx[:], ids.bitcast(U32).rearrange("(t p) f -> p t f", p=P)).then_inc(idx_in, 16)
                sp.dma_start(hot_ids[n % RING][:], ids_t[f:f + 1, :].broadcast_to([P, BATCH])) \
                    .then_inc(ids_in[n % RING], 16)
                sp.dma_start(hot_tab[n % RING][0:HOT_PARTS, 0:CHUNKS * D],
                             tables[f].rearrange("(p c) d -> p (c d)", c=CHUNKS)) \
                    .then_inc(hot_in[n % RING], 16)

            load_hot(0)
            load_hot(1)
            sp.dma_start(chunk_no[:], chunk_numbers.rearrange("a c s -> a (c s)").broadcast_to([P, CHUNKS * BATCH])
                         .rearrange("p (c s) -> p c s", c=CHUNKS)).then_inc(chunk_no_in, 16)
            sp.dma_start(rows[:, :, 0, :], x.rearrange("(t p) d -> p t d", p=P)).then_inc(dense_in, 16)
            load_hot(2)

            for n in range(RING, n_hot):
                load_hot(n)
            sp.dma_start(W1P[:], w1_pairs).then_inc(w1_in, 16)
            sp.dma_start(W1D[:], w1_dense).then_inc(w1_in, 16)
            sp.dma_start(W2[:], w2.rearrange("(c p) n -> p c n", p=P)).then_inc(w2_in, 16)
            with nc.allow_non_contiguous_dma(reason="a few hundred words of biases and W_top3"):
                sp.dma_start(W3[:], w3.rearrange("(c p) n -> p (c n)", p=P)).then_inc(w2_in, 16)
                sp.dma_start(B1[:], b1.rearrange("(c p) -> p c", p=P)).then_inc(bias_in, 16)
                sp.dma_start(B2[:], b2.rearrange("(c p) -> p c", p=P)).then_inc(bias_in, 16)
            sp.wait_ge(y_ready, TILES)
            sp.dma_start(out.rearrange("b o -> o b"), y[:]).then_inc(stored, 16)
            sp.wait_ge(stored, 16)

        @block.gpsimd
        def _(pool):
            pool.wait_ge(ident_zero, 1)
            pool.affine_select(out=ident[:], in_=ident[:], compare_op=ALU.not_equal, fill=1.0, base=0,
                               pattern=[[-1, P]], channel_multiplier=1).then_inc(ident_ready, 1)
            pool.iota(first_row_i[:], pattern=[[1, 1]], base=0, channel_multiplier=-CHUNKS).then_inc(iota_ready, 1)
            pool.wait_ge(idx_in, 16)
            pool.wait_ge(idx_in, 16)
            for t in range(TILES):
                for g in range(NG):
                    if t:
                        pool.wait_ge(gathered[g], 16 * gather_count(g) * t)
                    for s in GROUPS[g]:
                        if s:
                            f = SLOT_FIELD[s]
                            pool.indirect_dma_start(
                                rows[:, t, s, :], None, tables[f],
                                bass.IndirectOffsetOnAxis(ap=idx[:, t, f:f + 1], axis=0)).then_inc(gathered[g], 16)

        def empty_bank(eng, copy, i):
            eng.wait_ge(turned, i + 1)
            ps = fill_bank(i)
            item = fills[i]
            if item[0] == "hot":
                _, n, a, b = item
                copy(XT[:, a * P:b * P, TURNED + n], ps[:, 0:(b - a) * P]).then_inc(turn_read[reader[i]], 1)
                return
            _, t, g = item
            s0, n = GROUPS[g][0], len(GROUPS[g])
            here = slice(t * P, (t + 1) * P)
            if s0 == 0:
                copy(denseT[:, here], ps[:, 0:P])
            if g == NG - 1:
                copy(fewT[:, here], ps[0:SLOTS, n * P:(n + 1) * P])
            copy(XT[:, here, s0:s0 + n].rearrange("d s f -> d f s"),
                 ps[:, 0:n * P].rearrange("d (f s) -> d f s", f=n)).then_inc(turn_read[reader[i]], 1)

        def h1_out(t, n):
            if t == TILES - 1:
                return [h1_ps[:, 0, :], gram_ps[:, 0, 0:P], turn_ps[0][:, 0:P], turn_ps[1][:, 0:P]][n]
            return h1_ps[:, n, :]

        def h2_out(t, n):
            if t == TILES - 1 and n == 1:
                return gram_ps[:, 2, 0:P]
            return h2_ps[:, n * P:(n + 1) * P]

        def y_out(t):
            return gram_ps[0:1, 1, 0:P] if t == TILES - 1 else h2_ps[0:1, H2:H2 + P]

        def move_pairs(eng, copy, t, i, quads, done):
            eng.wait_ge(gram_ready, BATCHES * t + i + 1)
            banks = gram_ps[:, 2 * (i % 2):2 * (i % 2) + 2, 0:QUAD * QUAD * NCOL]
            b0 = t * P + i * BSAMP
            for j in quads:
                for s in range(4):
                    cols = slice(j * NCOL + s * PART_COLS, j * NCOL + (s + 1) * PART_COLS)
                    src = banks[32 * j:32 * j + 32].rearrange("a k (q n) -> a k q n", q=QUAD)[:, :, :, cols]
                    dst = PAIRS[32 * s:32 * s + 32, :, b0:b0 + BSAMP] \
                        .rearrange("a n (k q j) -> a k q j n", q=QUAD, j=QUAD)[:, :, :, j, :]
                    last = copy(dst, src)
            last.then_inc(done, 1)

        @block.scalar
        def _(act):
            def copy(dst, src):
                return nc.scalar.copy(dst, src)

            def relu1(t, n):
                nc.scalar.activation(h1[:, n, :], h1_out(t, n), ACT.Relu,
                                     bias=B1[:, n:n + 1]).then_inc(h1_ready, 1)

            def relu2(t, n):
                nc.scalar.activation(h2[:, n, :], h2_out(t, n), ACT.Relu,
                                     bias=B2[:, n:n + 1]).then_inc(h2_ready, 1)

            def keep_y(t):
                act.wait_ge(y_sum, t + 1)
                copy(y[0:1, t * P:(t + 1) * P], y_out(t)).then_inc(y_ready, 1)

            def chunk_of_ids(n):
                act.wait_ge(ids_in[n % RING], 16 * (n // RING + 1))
                if n >= 2:
                    act.wait_ge(onehot_ready, CHUNKS + n - 2)
                nc.scalar.activation(hot_chunk[n % 2][:], hot_ids[n % RING][:], ACT.Identity,
                                     bias=first_row[:, 0:1]).then_inc(chunk_ready, 1)

            act.wait_ge(first_row_ready, 1)
            chunk_of_ids(0)
            chunk_of_ids(1)
            for i in range(n_first):
                empty_bank(act, copy, i)
                if fills[i][0] == "hot" and fills[i][1] + 2 < n_hot:
                    chunk_of_ids(fills[i][1] + 2)
            act.wait_ge(bias_in, 32)
            for t in range(TILES):
                for i in range(BATCHES):
                    move_pairs(act, copy, t, i, (0, 1), pairs_act)
                    if t and i == 0:
                        keep_y(t - 1)
                if t == TILES - 1:
                    break
                for item in between[t]:
                    if reader[fill_no[item]] == "act":
                        empty_bank(act, copy, fill_no[item])
                act.wait_ge(h1_sum, t + 1)
                for n in range(HC1):
                    relu1(t, n)
                for k, item in enumerate(late[t]):
                    if reader[fill_no[item]] == "act":
                        empty_bank(act, copy, fill_no[item])
                    if k == 0:
                        act.wait_ge(h2_sum, t + 1)
                        for n in range(HC2):
                            relu2(t, n)
            for n in (0, 2):
                act.wait_ge(h1_sum, t + n + 1)
                relu1(t, n)
            act.wait_ge(h2_sum, t + 1)
            relu2(t, 0)
            keep_y(t)

        @block.vector
        def _(dve):
            def copy(dst, src):
                return nc.vector.tensor_copy(dst, src)

            def few_pairs(t):
                dve.wait_ge(cleared, 2)
                dve.wait_ge(dense_in, 16)
                dve.wait_ge(gathered[0], 16 * gather_count(0) * (t + 1))
                for i, (a, g) in enumerate(FEW):
                    if t or i:
                        dve.wait_ge(few_step, len(FEW) * t + i)
                    nc.vector.tensor_tensor_reduce(
                        out=few_prod[:], in0=rows[:, t, a, :], in1=rows[:, t, g, :], scale=1.0, scalar=0.0,
                        op0=ALU.mult, op1=ALU.add, accum_out=few[:, t, NVEC + i:NVEC + i + 1]).then_inc(few_step, 1)

            def add_few(t):
                here = slice(t * P, (t + 1) * P)
                dve.wait_ge(pairs_act, BATCHES * (t + 1))
                dve.wait_ge(pairs_dve, BATCHES * (t + 1))
                wait_emptied(dve, fill_no[("turn", t, NG - 1)])
                nc.vector.tensor_tensor(PAIRS[0:SLOTS, 0, here], PAIRS[0:SLOTS, 0, here], fewT[:, here],
                                        ALU.add).then_inc(pairs_full, 1)

            def relu_dve(t, n):
                dve.wait_ge(h1_sum, t + n + 1)
                nc.vector.tensor_scalar(h1[:, n, :], h1_out(t, n), B1[:, n:n + 1], 0.0,
                                        ALU.add, ALU.max).then_inc(h1_ready_dve, 1)

            def relu_last(t):
                dve.wait_ge(h2_sum, t + 2)
                nc.vector.tensor_scalar(h2[:, 1, :], h2_out(t, 1), B2[:, 1:2], 0.0,
                                        ALU.add, ALU.max).then_inc(h2_ready_dve, 1)

            nc.vector.memset(ident[:], 0.0).then_inc(ident_zero, 1)
            nc.vector.memset(few[:], 0.0).then_inc(cleared, 1)
            dve.wait_ge(iota_ready, 1)
            copy(first_row[:], first_row_i[:]).then_inc(first_row_ready, 1)
            nc.vector.memset(XT[:, :, NVEC:SLOTS], 0.0).then_inc(cleared, 1)
            part = slice(0, HOT_PARTS)
            for n in range(n_hot):
                b = n % 2
                tab = hot_tab[n % RING][part, :]
                if n >= 2:
                    dve.wait_ge(turned, hot_done(n - 2))
                dve.wait_ge(chunk_ready, n + 1)
                if n == 0:
                    for k in range(CHUNKS):
                        nc.vector.tensor_scalar(onehot[b][part, k, :], hot_chunk[b][part, :], float(k), None,
                                                ALU.is_equal).then_inc(onehot_ready, 1)
                else:
                    dve.wait_ge(chunk_no_in, 16)
                    nc.vector.tensor_tensor(
                        onehot[b][part, :, :],
                        hot_chunk[b][part, :].rearrange("p (a s) -> p a s", a=1).broadcast_to([HOT_PARTS, CHUNKS, BATCH]),
                        chunk_no[part, :, :], ALU.is_equal).then_inc(onehot_ready, 1)
                dve.wait_ge(hot_in[n % RING], 16 * (n // RING + 1))
                high = tab.bitcast(BF16)[:, 1::2]
                nc.vector.tensor_tensor(hot_rest[b][part, :], tab, high, ALU.subtract).then_inc(rest_ready, 1)
                dve.wait_ge(rest_ready, n + 1)
                mid = hot_rest[b][part, :].bitcast(BF16)[:, 1::2]
                nc.vector.tensor_tensor(hot_low[b][part, :], hot_rest[b][part, :], mid,
                                        ALU.subtract).then_inc(low_ready, 1)
                if n == 2:
                    few_pairs(0)
            for t in range(TILES):
                for i in range(BATCHES):
                    move_pairs(dve, copy, t, i, (2, 3), pairs_dve)
                add_few(t)
                if t == TILES - 1:
                    break
                for k, item in enumerate(between[t] + late[t]):
                    if reader[fill_no[item]] == "dve":
                        empty_bank(dve, copy, fill_no[item])
                    if k == 1:
                        few_pairs(t + 1)
            relu_dve(t, 1)
            relu_dve(t, 3)
            relu_last(t)

        @block.tensor
        def _(pe):
            pe.wait_ge(ident_ready, 1)
            for _ in range(WARM_UP):
                nc.tensor.matmul(h2_ps[:, 0:P], ident[:], ident[:], start=True, stop=True)

            def bank_free(i):
                if bank_before(i) >= 0:
                    wait_emptied(pe, bank_before(i))

            def fill(item):
                i = fill_no[item]
                ps = fill_bank(i)
                bank_free(i)
                if item[0] == "hot":
                    _, n, lo, hi = item
                    b, c = n % 2, CHUNKS
                    ps = ps[:, 0:(hi - lo) * P]
                    part = slice(0, HOT_PARTS)
                    words = [hot_tab[n % RING][part, :].bitcast(BF16), hot_rest[b][part, :].bitcast(BF16)]
                    if n:
                        pe.wait_ge(onehot_ready, CHUNKS + n)
                    pe.wait_ge(hot_in[n % RING], 16 * (n // RING + 1))
                    for which in range(3):
                        if which == 1:
                            pe.wait_ge(rest_ready, n + 1)
                        if which == 2:
                            pe.wait_ge(low_ready, n + 1)
                        for k in range(c):
                            if n == 0 and which == 0:
                                pe.wait_ge(onehot_ready, k + 1)
                            if which < 2:
                                w = words[which][:, 2 * k * D + 1:2 * (k + 1) * D:2]
                            else:
                                w = hot_low[b][part, k * D:(k + 1) * D]
                            last = nc.tensor.matmul(ps, w, onehot[b][part, k, lo * P:hi * P],
                                                    start=(which == 0 and k == 0), stop=(which == 2 and k == c - 1))
                    last.then_inc(turned, 1)
                    return
                _, t, g = item
                if gather_count(g):
                    pe.wait_ge(gathered[g], 16 * gather_count(g) * (t + 1))
                if GROUPS[g][0] == 0:
                    pe.wait_ge(dense_in, 16)
                for k, s in enumerate(GROUPS[g]):
                    last = nc.tensor.transpose(ps[:, k * P:(k + 1) * P], rows[:, t, s, :], ident[:])
                if g == NG - 1:
                    pe.wait_ge(few_step, len(FEW) * (t + 1))
                    n = len(GROUPS[g])
                    last = nc.tensor.transpose(ps[0:SLOTS, n * P:(n + 1) * P], few[:, t, :], ident[:])
                last.then_inc(turned, 1)

            def gram(t, i):
                if i == 0:
                    wait_emptied(pe, max(n_first - 1, fills_for_tile(t)))
                b = BATCHES * t + i
                if b >= 2:
                    pe.wait_ge(pairs_act, b - 1)
                    pe.wait_ge(pairs_dve, b - 1)
                for q in range(BSAMP // QUAD):
                    s0 = t * P + i * BSAMP + q * QUAD
                    four = XT[:, s0:s0 + QUAD, :]
                    o = (q % QUAD) * QUAD * NCOL
                    last = nc.tensor.matmul(gram_ps[:, 2 * (i % 2) + q // QUAD, o:o + QUAD * NCOL],
                                            four.rearrange("d s f -> d (s f)"), four[:, :, FIRST:NVEC],
                                            start=True, stop=True)
                last.then_inc(gram_ready, 1)

            def layer1_dense(t, n):
                nc.tensor.matmul(h1_out(t, n), W1D[:, n * P:(n + 1) * P], denseT[:, t * P:(t + 1) * P],
                                 start=True, stop=False)

            def layer1_pairs(t, n):
                for k in range(PART_COLS):
                    last = nc.tensor.matmul(h1_out(t, n), W1P[:, k, n * P:(n + 1) * P], PAIRS[:, k, t * P:(t + 1) * P],
                                            start=False, stop=(k == PART_COLS - 1))
                if t == TILES - 1 or n == HC1 - 1:
                    last.then_inc(h1_sum, 1)

            def layer2(t):
                if t:
                    pe.wait_ge(y_ready, t)
                for n in range(HC2):
                    for k in range(HC1):
                        if n == 0 and t < TILES - 1:
                            pe.wait_ge(h1_ready, HC1 * t + k + 1)
                        elif n == 0 and k % 2 == 0:
                            pe.wait_ge(h1_ready, HC1 * t + k // 2 + 1)
                        elif n == 0:
                            pe.wait_ge(h1_ready_dve, k // 2 + 1)
                        last = nc.tensor.matmul(h2_out(t, n), W2[:, k, n * P:(n + 1) * P],
                                                h1[:, k, :], start=(k == 0), stop=(k == HC1 - 1))
                    if t == TILES - 1 or n == HC2 - 1:
                        last.then_inc(h2_sum, 1)

            def layer3(t):
                final = t == TILES - 1
                for k in range(HC2):
                    if final and k == 1:
                        pe.wait_ge(h2_ready_dve, 1)
                    elif k == 0:
                        pe.wait_ge(h2_ready, HC2 * t + (1 if final else HC2))
                    last = nc.tensor.matmul(y_out(t), W3[:, k:k + 1], h2[:, k, :],
                                            start=(k == 0), stop=(k == HC2 - 1))
                last.then_inc(y_sum, 1)

            for item in fills[:n_first]:
                fill(item)
            pe.wait_ge(w1_in, 32)
            pe.wait_ge(w2_in, 32)
            pe.wait_ge(cleared, 2)
            for t in range(TILES):
                for i in range(BATCHES):
                    gram(t, i)
                    if t and i == 0:
                        layer3(t - 1)
                if t == TILES - 1:
                    break
                fill(between[t][0])
                if t:
                    pe.wait_ge(h1_ready, HC1 * t)
                for n in range(HC1):
                    layer1_dense(t, n)
                    if n == 0:
                        pe.wait_ge(pairs_full, t + 1)
                    layer1_pairs(t, n)
                    for item in between[t][n + 1:n + 2]:
                        fill(item)
                fill(late[t][0])
                layer2(t)
                for item in late[t][1:]:
                    fill(item)
            pe.wait_ge(pairs_act, BATCHES * (t + 1) - 1)
            pe.wait_ge(pairs_dve, BATCHES * (t + 1) - 1)
            for n in range(HC1):
                layer1_dense(t, n)
            pe.wait_ge(pairs_full, t + 1)
            for n in range(HC1):
                layer1_pairs(t, n)
            layer2(t)
            layer3(t)


def pair_rows():
    rows = []
    slot = {f: s for s, f in enumerate(SLOT_FIELD)}
    n = 0
    for i in range(NVEC):
        for j in range(i + 1, NVEC):
            a, g = sorted((slot[i], slot[j]))
            if g < FIRST:
                rows.append((NVEC + FEW.index((a, g)), 0, n))
            else:
                s, k = divmod(g - FIRST, PART_COLS)
                rows.append((32 * s + a, k, n))
            n += 1
    return rows, n


def kernel(**inputs):
    import numpy as _np
    import concourse.bacc as _bacc
    from concourse import mybir as _mybir
    from concourse.bass_utils import run_bass_kernel_spmd as _run

    nc = _bacc.Bacc("TRN2", target_bir_lowering=False, num_devices=1)
    arrays, args = {}, {}

    def give(name, a):
        a = _np.ascontiguousarray(a)
        arrays[f"in_{name}_dram"] = a
        args[name] = nc.dram_tensor(f"in_{name}_dram", a.shape, _mybir.dt.from_np(a.dtype), kind="ExternalInput").ap()
        return args[name]

    x = give("r_dense_x", inputs["r_dense_x"])
    ids = give("ids", inputs["ids"])
    ids_t = give("ids_t", _np.asarray(inputs["ids"]).T)
    chunk_numbers = give("chunk_numbers", _np.repeat(_np.arange(CHUNKS, dtype=_np.float16), BATCH)
                         .reshape(1, CHUNKS, BATCH))
    tables = [give(f"tbl_{f}", inputs[f"tbl_{f}"]) for f in range(NTAB)]
    w1 = _np.asarray(inputs["W_top1"])
    where, n_pairs = pair_rows()
    p, k, r = (_np.array(c) for c in zip(*where))
    w1_pairs = _np.zeros((P, PART_COLS, H1), w1.dtype)
    w1_pairs[p, k] = w1[r]
    w1p = give("w1_pairs", w1_pairs)
    w1d = give("w1_dense", w1[n_pairs:])
    b1 = give("b_top1", inputs["b_top1"])
    w2 = give("W_top2", inputs["W_top2"])
    b2 = give("b_top2", inputs["b_top2"])
    w3 = give("W_top3", inputs["W_top3"])
    out = nc.dram_tensor("out_0_dram", (BATCH, 1), _mybir.dt.float32, kind="ExternalOutput").ap()
    build(nc, x, ids, ids_t, chunk_numbers, tables, w1p, w1d, b1, w2, b2, w3, out)
    r = _run(nc, [arrays], core_ids=[0])
    return r.results[0]["out_0_dram"]
```

```python
from contextlib import ExitStack

import concourse.bass as bass
from concourse import mybir

F32 = mybir.dt.float32
F16 = mybir.dt.float16
BF16 = mybir.dt.bfloat16
U32 = mybir.dt.uint32
I32 = mybir.dt.int32
ALU = mybir.AluOpType
ACT = mybir.ActivationFunctionType

P = 128
BATCH = 512
D = 128
TILES = BATCH // P
NTAB = 26
NVEC = NTAB + 1
SLOTS = 32
FIRST = 7
FEW = [(a, g) for g in range(FIRST) for a in range(g)]
QUAD = 4
NCOL = NVEC - FIRST
PART_COLS = NCOL // 4
BATCHES = 4
BSAMP = P // BATCHES
SPARE = SLOTS - NVEC
FEW_PER_CHUNK = 4 * SPARE
FEW_CHUNKS = -(-len(FEW) // FEW_PER_CHUNK)
FEW_COLS = (FEW_CHUNKS - 1) * P + SLOTS
FEW_PARTS = 3
FEW_GO = len(FEW) // FEW_PARTS
assert len(FEW) == FEW_PARTS * FEW_GO and FEW_CHUNKS == 2 and len(FEW) - FEW_PER_CHUNK <= SPARE
GRAM_ROWS = SLOTS * (QUAD - 1) + NVEC
H1, H2 = 512, 256
HC1, HC2 = H1 // P, H2 // P
BANK = 512
WARM_UP = 9
PER_TILE = 2
LATE = 3
BEFORE_L2 = [LATE + PER_TILE - 1] * (TILES - 2) + [1]
RING = 3

HOT = [1, 5, 7, 9, 12]
HOT_ROWS = 1000
HOT_PARTS = 125
CHUNKS = HOT_ROWS // HOT_PARTS
COLD = [f for f in range(NTAB) if f not in HOT]
GROUP_SIZES = [3, 4, 4, 4, 4, 2, 1]
SLOT_FIELD = [NTAB] + COLD + HOT
TURNED = 1 + len(COLD)
GROUPS = [list(range(sum(GROUP_SIZES[:g]), sum(GROUP_SIZES[:g + 1]))) for g in range(len(GROUP_SIZES))]
assert GROUPS[-1][-1] == TURNED - 1
NG = len(GROUPS)
FEW_AFTER = 2


def build(nc, x, ids, ids_t, chunk_numbers, tables, w1_pairs, w1_dense, b1, w2, b2, w3, out):
    n_hot = len(HOT)
    assert all(tables[f].shape[0] == HOT_ROWS for f in HOT)

    with ExitStack() as ctx:
        def sb(name, shape, dt):
            return ctx.enter_context(nc.sbuf_tensor(name, shape, dt))

        def psum(name, shape, dt=F32):
            return ctx.enter_context(nc.psum_tensor(name, shape, dt))

        def sem(name):
            return ctx.enter_context(nc.semaphore(name))

        idx = sb("idx", [P, TILES, NTAB], U32)
        rows = sb("rows", [P, TILES, TURNED, D], F32)
        ident = sb("ident", [P, P], F32)
        XT = sb("XT", [P, BATCH, SLOTS], F32)
        denseT = sb("denseT", [P, BATCH], F32)
        few = sb("few", [P, TILES, FEW_COLS], F32)
        few_prod = sb("few_prod", [P, 2, D], F32)
        PAIRS = sb("PAIRS", [P, PART_COLS, BATCH], F32)
        W1P = sb("W1P", [P, PART_COLS, H1], F32)
        W1D = sb("W1D", [P, H1], F32)
        W2 = sb("W2", [P, HC1, H2], F32)
        W3 = sb("W3", [P, HC2], F32)
        B1 = sb("B1", [P, HC1], F32)
        B2 = sb("B2", [P, HC2], F32)
        h1 = sb("h1", [P, HC1, P], F32)
        h2 = sb("h2", [P, HC2, P], F32)
        y = sb("y", [1, BATCH], F32)
        hot_tab = [sb(f"hot_tab{i}", [P, CHUNKS * D], F32) for i in range(RING)]
        hot_rest = [sb(f"hot_rest{i}", [P, CHUNKS * D], F32) for i in range(2)]
        hot_low = [sb(f"hot_low{i}", [P, CHUNKS * D], BF16) for i in range(2)]
        hot_ids = [sb(f"hot_ids{i}", [P, BATCH], I32) for i in range(RING)]
        hot_chunk = [sb(f"hot_chunk{i}", [P, BATCH], F16) for i in range(2)]
        chunk_no = sb("chunk_no", [P, CHUNKS, BATCH], F16)
        onehot = [sb(f"onehot{i}", [P, CHUNKS, BATCH], BF16) for i in range(2)]
        first_row_i = sb("first_row_i", [P, 1], I32)
        first_row = sb("first_row", [P, 1], F32)

        turn_ps = [psum(f"turn_ps{i}", [P, BANK]) for i in range(2)]
        gram_ps = psum("gram_ps", [P, 4, BANK])
        h1_ps = psum("h1_ps", [P, HC1, P])
        h2_ps = psum("h2_ps", [P, BANK])

        idx_in = sem("idx_in")
        dense_in = sem("dense_in")
        w1_in = sem("w1_in")
        w2_in = sem("w2_in")
        bias_in = sem("bias_in")
        hot_in = [sem(f"hot_in{i}") for i in range(RING)]
        ids_in = [sem(f"ids_in{i}") for i in range(RING)]
        gathered = [sem(f"gathered{g}") for g in range(NG)]
        ident_zero = sem("ident_zero")
        ident_ready = sem("ident_ready")
        iota_ready = sem("iota_ready")
        first_row_ready = sem("first_row_ready")
        chunk_no_in = sem("chunk_no_in")
        padding_clear = sem("padding_clear")
        few_cleared = sem("few_cleared")
        rest_ready = sem("rest_ready")
        low_ready = sem("low_ready")
        chunk_ready = sem("chunk_ready")
        onehot_ready = sem("onehot_ready")
        turned = sem("turned")
        turn_read = {"act": sem("turn_read_act"), "dve": sem("turn_read_dve")}
        gram_ready = sem("gram_ready")
        few_step = sem("few_step")
        pairs_zero = sem("pairs_zero")
        pairs_act = sem("pairs_act")
        pairs_dve = sem("pairs_dve")
        h1_sum = sem("h1_sum")
        h1_ready = sem("h1_ready")
        h2_sum = sem("h2_sum")
        h2_ready = sem("h2_ready")
        h1_ready_dve = sem("h1_ready_dve")
        h2_ready_dve = sem("h2_ready_dve")
        y_sum = sem("y_sum")
        y_ready = sem("y_ready")
        stored = sem("stored")
        block = ctx.enter_context(nc.Block())

        whole, by_tile = range(n_hot - PER_TILE), range(n_hot - PER_TILE, n_hot)
        fills, early = [], [("turn", 0, g) for g in range(NG)]
        for n in whole:
            fills.append(("hot", n, 0, TILES))
            if n:
                fills.append(early.pop(0))
        for n in by_tile:
            fills += [early.pop(0), ("hot", n, 0, 1)]
        fills += early
        n_first = len(fills)
        between = [[] for _ in range(TILES)]
        late = [[] for _ in range(TILES)]
        for t in range(TILES - 1):
            turns = [("turn", t + 1, g) for g in range(NG)]
            hots = [("hot", n, t + 1, t + 2) for n in by_tile]
            between[t] = hots[:1] + turns[:-LATE]
            late[t] = hots[1:] + turns[-LATE:]
        for t in range(TILES):
            fills += [("few", t)] + between[t] + late[t]
        fill_no = {item: i for i, item in enumerate(fills)}
        shared = between[0] + sum(late, [])
        reader = ["act" if i < n_first or item in shared[1::2] else "dve" for i, item in enumerate(fills)]
        few_bank = {t: turn_ps[fill_no[("few", t)] % 2] for t in range(TILES)}
        other_bank = turn_ps[1 - fill_no[("few", TILES - 1)] % 2]

        def fill_bank(i):
            early = [turn_ps[0][:], turn_ps[1][:], gram_ps[:, 0, :], gram_ps[:, 1, :]]
            return early[i % 4] if i < n_first else turn_ps[i % 2][:]

        def bank_before(i):
            if i < n_first:
                return i - 4
            return max([j for j in range(n_first) if j % 4 == i % 2], default=-1) if i - 2 < n_first else i - 2

        def wait_emptied(eng, upto):
            for who in ("act", "dve"):
                count = reader[:upto + 1].count(who)
                if count:
                    eng.wait_ge(turn_read[who], count)

        def fills_for_tile(t):
            return max(i for i, item in enumerate(fills)
                       if (item[2] <= t < item[3] if item[0] == "hot" else item[0] == "turn" and item[1] == t))

        def hot_done(n):
            return max(i for i, item in enumerate(fills) if item[:2] == ("hot", n)) + 1

        def gather_count(g):
            return sum(1 for s in GROUPS[g] if s > 0)

        @block.sync
        def _(sp):
            def load_hot(n):
                if n >= RING:
                    sp.wait_ge(turned, hot_done(n - RING))
                f = HOT[n]
                sp.dma_start(hot_ids[n % RING][:], ids_t[f:f + 1, :].broadcast_to([P, BATCH])) \
                    .then_inc(ids_in[n % RING], 16)
                sp.dma_start(hot_tab[n % RING][0:HOT_PARTS, 0:CHUNKS * D],
                             tables[f].rearrange("(p c) d -> p (c d)", c=CHUNKS)) \
                    .then_inc(hot_in[n % RING], 16)

            sp.dma_start(idx[:], ids.bitcast(U32).rearrange("(t p) f -> p t f", p=P)).then_inc(idx_in, 16)
            load_hot(0)
            sp.dma_start(chunk_no[:], chunk_numbers.rearrange("a c s -> a (c s)").broadcast_to([P, CHUNKS * BATCH])
                         .rearrange("p (c s) -> p c s", c=CHUNKS)).then_inc(chunk_no_in, 16)
            load_hot(1)
            sp.dma_start(rows[:, :, 0, :], x.rearrange("(t p) d -> p t d", p=P)).then_inc(dense_in, 16)
            for n in range(2, n_hot):
                load_hot(n)
            sp.dma_start(W1P[:], w1_pairs).then_inc(w1_in, 16)
            sp.dma_start(W1D[:], w1_dense).then_inc(w1_in, 16)
            sp.dma_start(W2[:], w2.rearrange("(c p) n -> p c n", p=P)).then_inc(w2_in, 16)
            with nc.allow_non_contiguous_dma(reason="a few hundred words of biases and W_top3"):
                sp.dma_start(W3[:], w3.rearrange("(c p) n -> p (c n)", p=P)).then_inc(w2_in, 16)
                sp.dma_start(B1[:], b1.rearrange("(c p) -> p c", p=P)).then_inc(bias_in, 16)
                sp.dma_start(B2[:], b2.rearrange("(c p) -> p c", p=P)).then_inc(bias_in, 16)
            sp.wait_ge(y_ready, TILES)
            sp.dma_start(out.rearrange("b o -> o b"), y[:]).then_inc(stored, 16)
            sp.wait_ge(stored, 16)

        @block.gpsimd
        def _(pool):
            pool.wait_ge(ident_zero, 1)
            pool.affine_select(out=ident[:], in_=ident[:], compare_op=ALU.not_equal, fill=1.0, base=0,
                               pattern=[[-1, P]], channel_multiplier=1).then_inc(ident_ready, 1)
            pool.iota(first_row_i[:], pattern=[[1, 1]], base=0, channel_multiplier=-CHUNKS).then_inc(iota_ready, 1)
            nc.gpsimd.memset(few[:], 0.0).then_inc(few_cleared, 1)
            pool.wait_ge(idx_in, 16)
            for t in range(TILES):
                for g in range(NG):
                    if t:
                        pool.wait_ge(gathered[g], 16 * gather_count(g) * t)
                    for s in GROUPS[g]:
                        if s:
                            f = SLOT_FIELD[s]
                            pool.indirect_dma_start(
                                rows[:, t, s, :], None, tables[f],
                                bass.IndirectOffsetOnAxis(ap=idx[:, t, f:f + 1], axis=0)) \
                                .then_inc(gathered[g], 16)

        def empty_bank(eng, copy, i):
            eng.wait_ge(turned, i + 1)
            ps = fill_bank(i)
            item = fills[i]
            if item[0] == "hot":
                _, n, a, b = item
                copy(XT[:, a * P:b * P, TURNED + n], ps[:, 0:(b - a) * P]).then_inc(turn_read[reader[i]], 1)
                return
            _, t, g = item
            s0, n = GROUPS[g][0], len(GROUPS[g])
            here = slice(t * P, (t + 1) * P)
            if s0 == 0:
                copy(denseT[:, here], ps[:, 0:P])
            copy(XT[:, here, s0:s0 + n].rearrange("d s f -> d f s"),
                 ps[:, 0:n * P].rearrange("d (f s) -> d f s", f=n)).then_inc(turn_read[reader[i]], 1)

        def h1_out(t, n):
            if t == TILES - 1:
                return [h1_ps[:, 0, :], gram_ps[:, 0, 0:P], other_bank[:, 0:P], few_bank[t][:, 0:P]][n]
            return h1_ps[:, n, :]

        def h2_out(t, n):
            if t == TILES - 1 and n == 1:
                return gram_ps[:, 2, 0:P]
            return h2_ps[:, n * P:(n + 1) * P]

        def y_out(t):
            return gram_ps[0:1, 1, 0:P] if t == TILES - 1 else h2_ps[0:1, H2:H2 + P]

        def move_pairs(eng, copy, t, i, quads, done):
            eng.wait_ge(gram_ready, BATCHES * t + i + 1)
            banks = gram_ps[:, 2 * (i % 2):2 * (i % 2) + 2, 0:QUAD * QUAD * NCOL]
            b0 = t * P + i * BSAMP
            for j in quads:
                for s in range(4):
                    cols = slice(j * NCOL + s * PART_COLS, j * NCOL + (s + 1) * PART_COLS)
                    src = banks[32 * j:32 * j + NVEC].rearrange("a k (q n) -> a k q n", q=QUAD)[:, :, :, cols]
                    dst = PAIRS[32 * s:32 * s + NVEC, :, b0:b0 + BSAMP] \
                        .rearrange("a n (k q j) -> a k q j n", q=QUAD, j=QUAD)[:, :, :, j, :]
                    last = copy(dst, src)
            last.then_inc(done, 1)

        @block.scalar
        def _(act):
            def copy(dst, src):
                return nc.scalar.copy(dst, src)

            def relu1(t, n):
                nc.scalar.activation(h1[:, n, :], h1_out(t, n), ACT.Relu,
                                     bias=B1[:, n:n + 1]).then_inc(h1_ready, 1)

            def relu2(t, n):
                nc.scalar.activation(h2[:, n, :], h2_out(t, n), ACT.Relu,
                                     bias=B2[:, n:n + 1]).then_inc(h2_ready, 1)

            def keep_y(t):
                act.wait_ge(y_sum, t + 1)
                copy(y[0:1, t * P:(t + 1) * P], y_out(t)).then_inc(y_ready, 1)

            def chunk_of_ids(n):
                act.wait_ge(ids_in[n % RING], 16 * (n // RING + 1))
                if n >= 2:
                    act.wait_ge(onehot_ready, CHUNKS + n - 2)
                nc.scalar.activation(hot_chunk[n % 2][:], hot_ids[n % RING][:], ACT.Identity,
                                     bias=first_row[:, 0:1]).then_inc(chunk_ready, 1)

            def zero_pairs(a, b):
                zeros = few[:, 0:1, 0:P].broadcast_to([P, b - a, P])
                for c in range(TILES):
                    cols = slice(c * P, (c + 1) * P)
                    last = nc.scalar.activation(PAIRS[:, a:b, cols], zeros, ACT.Identity)
                last.then_inc(pairs_zero, 1)

            act.wait_ge(few_cleared, 1)
            zero_pairs(0, PART_COLS // 2)
            act.wait_ge(first_row_ready, 1)
            chunk_of_ids(0)
            chunk_of_ids(1)
            zero_pairs(PART_COLS // 2, PART_COLS)
            for i in range(n_first):
                empty_bank(act, copy, i)
                if fills[i][0] == "hot" and fills[i][1] + 2 < n_hot:
                    chunk_of_ids(fills[i][1] + 2)
            act.wait_ge(bias_in, 32)
            for t in range(TILES):
                for i in range(BATCHES):
                    move_pairs(act, copy, t, i, (0, 1), pairs_act)
                    if 0 < t < TILES - 1 and i == 0:
                        keep_y(t - 1)
                if t == TILES - 1:
                    break
                for item in between[t]:
                    if reader[fill_no[item]] == "act":
                        empty_bank(act, copy, fill_no[item])
                act.wait_ge(h1_sum, t + 1)
                for n in range(HC1):
                    relu1(t, n)
                for k, item in enumerate(late[t]):
                    if t == TILES - 2 and item is late[t][-1]:
                        keep_y(t)
                    if reader[fill_no[item]] == "act":
                        empty_bank(act, copy, fill_no[item])
                    if k == BEFORE_L2[t] - 1:
                        act.wait_ge(h2_sum, t + 1)
                        for n in range(HC2):
                            relu2(t, n)
            for n in (0, 2):
                act.wait_ge(h1_sum, t + n + 1)
                relu1(t, n)
            act.wait_ge(h2_sum, t + 1)
            relu2(t, 0)
            keep_y(t)

        @block.vector
        def _(dve):
            def copy(dst, src):
                return nc.vector.tensor_copy(dst, src)

            def few_pairs(t, part):
                if part == 0:
                    dve.wait_ge(few_cleared, 1)
                    if t == 0:
                        dve.wait_ge(pairs_zero, 2)
                    dve.wait_ge(dense_in, 16)
                for g in range(NG):
                    if GROUPS[g][0] < FIRST:
                        dve.wait_ge(gathered[g], 16 * gather_count(g) * (t + 1))
                for i in range(part * FEW_GO, (part + 1) * FEW_GO):
                    a, g = FEW[i]
                    step = len(FEW) * t + i
                    if step >= 2:
                        dve.wait_ge(few_step, step - 1)
                    col = few_place(i)[1] * P + few_place(i)[0]
                    nc.vector.tensor_tensor_reduce(
                        out=few_prod[:, step % 2, :], in0=rows[:, t, a, :], in1=rows[:, t, g, :], scale=1.0,
                        scalar=0.0, op0=ALU.mult, op1=ALU.add,
                        accum_out=few[:, t, col:col + 1]).then_inc(few_step, 1)

            def add_few(t):
                here = slice(t * P, (t + 1) * P)
                dve.wait_ge(pairs_act, BATCHES * (t + 1))
                dve.wait_ge(pairs_dve, BATCHES * (t + 1))
                dve.wait_ge(turned, fill_no[("few", t)] + 1)
                nc.vector.tensor_tensor(PAIRS[:, 0, here], PAIRS[:, 0, here], few_bank[t][:, 0:P], ALU.add)
                nc.vector.tensor_tensor(PAIRS[0:SLOTS, 1, here], PAIRS[0:SLOTS, 1, here],
                                        few_bank[t][0:SLOTS, P:2 * P], ALU.add).then_inc(turn_read["dve"], 1)

            def relu_dve(t, n):
                dve.wait_ge(h1_sum, t + n + 1)
                nc.vector.tensor_scalar(h1[:, n, :], h1_out(t, n), B1[:, n:n + 1], 0.0,
                                        ALU.add, ALU.max).then_inc(h1_ready_dve, 1)

            def relu_last(t):
                dve.wait_ge(h2_sum, t + 2)
                nc.vector.tensor_scalar(h2[:, 1, :], h2_out(t, 1), B2[:, 1:2], 0.0,
                                        ALU.add, ALU.max).then_inc(h2_ready_dve, 1)

            nc.vector.memset(ident[:], 0.0).then_inc(ident_zero, 1)
            dve.wait_ge(iota_ready, 1)
            copy(first_row[:], first_row_i[:]).then_inc(first_row_ready, 1)
            nc.vector.memset(XT[:, :, NVEC:SLOTS], 0.0).then_inc(padding_clear, 1)
            part = slice(0, HOT_PARTS)
            for n in range(n_hot):
                b = n % 2
                tab = hot_tab[n % RING][part, :]
                if n >= 2:
                    dve.wait_ge(turned, hot_done(n - 2))
                dve.wait_ge(chunk_ready, n + 1)
                if n == 0:
                    for k in range(CHUNKS):
                        nc.vector.tensor_scalar(onehot[b][part, k, :], hot_chunk[b][part, :], float(k), None,
                                                ALU.is_equal).then_inc(onehot_ready, 1)
                else:
                    dve.wait_ge(chunk_no_in, 16)
                    nc.vector.tensor_tensor(
                        onehot[b][part, :, :],
                        hot_chunk[b][part, :].rearrange("p (a s) -> p a s", a=1)
                        .broadcast_to([HOT_PARTS, CHUNKS, BATCH]),
                        chunk_no[part, :, :], ALU.is_equal).then_inc(onehot_ready, 1)
                dve.wait_ge(hot_in[n % RING], 16 * (n // RING + 1))
                high = tab.bitcast(BF16)[:, 1::2]
                nc.vector.tensor_tensor(hot_rest[b][part, :], tab, high, ALU.subtract).then_inc(rest_ready, 1)
                dve.wait_ge(rest_ready, n + 1)
                mid = hot_rest[b][part, :].bitcast(BF16)[:, 1::2]
                nc.vector.tensor_tensor(hot_low[b][part, :], hot_rest[b][part, :], mid,
                                        ALU.subtract).then_inc(low_ready, 1)
            for part in range(FEW_PARTS):
                few_pairs(0, part)
            for t in range(TILES):
                for i in range(BATCHES):
                    move_pairs(dve, copy, t, i, (2, 3), pairs_dve)
                add_few(t)
                if t == TILES - 1:
                    break
                for k, item in enumerate(between[t] + late[t]):
                    if reader[fill_no[item]] == "dve":
                        empty_bank(dve, copy, fill_no[item])
                    if 1 <= k <= FEW_PARTS:
                        few_pairs(t + 1, k - 1)
            dve.wait_ge(bias_in, 32)
            relu_dve(t, 1)
            relu_dve(t, 3)
            relu_last(t)

        @block.tensor
        def _(pe):
            pe.wait_ge(ident_ready, 1)
            for _ in range(WARM_UP):
                nc.tensor.matmul(h2_ps[:, 0:P], ident[:], ident[:], start=True, stop=True)

            def bank_free(i):
                if bank_before(i) >= 0:
                    wait_emptied(pe, bank_before(i))

            def fill(item):
                i = fill_no[item]
                ps = fill_bank(i)
                bank_free(i)
                if item[0] == "hot":
                    _, n, lo, hi = item
                    b = n % 2
                    ps = ps[:, 0:(hi - lo) * P]
                    part = slice(0, HOT_PARTS)
                    words = [hot_tab[n % RING][part, :].bitcast(BF16), hot_rest[b][part, :].bitcast(BF16)]
                    if n:
                        pe.wait_ge(onehot_ready, CHUNKS + n)
                    pe.wait_ge(hot_in[n % RING], 16 * (n // RING + 1))
                    for which in range(3):
                        if which == 1:
                            pe.wait_ge(rest_ready, n + 1)
                        if which == 2:
                            pe.wait_ge(low_ready, n + 1)
                        for k in range(CHUNKS):
                            if n == 0 and which == 0:
                                pe.wait_ge(onehot_ready, k + 1)
                            if which < 2:
                                w = words[which][:, 2 * k * D + 1:2 * (k + 1) * D:2]
                            else:
                                w = hot_low[b][part, k * D:(k + 1) * D]
                            last = nc.tensor.matmul(ps, w, onehot[b][part, k, lo * P:hi * P],
                                                    start=(which == 0 and k == 0), stop=(which == 2 and k == CHUNKS - 1))
                    last.then_inc(turned, 1)
                    return
                _, t, g = item
                if gather_count(g):
                    pe.wait_ge(gathered[g], 16 * gather_count(g) * (t + 1))
                if GROUPS[g][0] == 0:
                    pe.wait_ge(dense_in, 16)
                for k, s in enumerate(GROUPS[g]):
                    last = nc.tensor.transpose(ps[:, k * P:(k + 1) * P], rows[:, t, s, :], ident[:])
                last.then_inc(turned, 1)

            def turn_few(t):
                i = fill_no[("few", t)]
                bank_free(i)
                pe.wait_ge(few_step, len(FEW) * (t + 1))
                nc.tensor.transpose(few_bank[t][:, 0:P], few[:, t, 0:P], ident[:])
                nc.tensor.transpose(few_bank[t][0:SLOTS, P:2 * P], few[:, t, P:FEW_COLS], ident[:]).then_inc(turned, 1)

            def gram(t, i):
                if i == 0:
                    wait_emptied(pe, max(n_first - 1, fills_for_tile(t)))
                b = BATCHES * t + i
                if b >= 2:
                    pe.wait_ge(pairs_act, b - 1)
                    pe.wait_ge(pairs_dve, b - 1)
                for q in range(BSAMP // QUAD):
                    s0 = t * P + i * BSAMP + q * QUAD
                    four = XT[:, s0:s0 + QUAD, :]
                    o = (q % QUAD) * QUAD * NCOL
                    last = nc.tensor.matmul(gram_ps[0:GRAM_ROWS, 2 * (i % 2) + q // QUAD, o:o + QUAD * NCOL],
                                            four.rearrange("d s f -> d (s f)")[:, 0:GRAM_ROWS], four[:, :, FIRST:NVEC],
                                            start=True, stop=True)
                last.then_inc(gram_ready, 1)

            def layer1_dense(t, n):
                nc.tensor.matmul(h1_out(t, n), W1D[:, n * P:(n + 1) * P], denseT[:, t * P:(t + 1) * P],
                                 start=True, stop=False)

            def layer1_pairs(t, n):
                order = list(range(FEW_CHUNKS, PART_COLS)) + list(range(FEW_CHUNKS))
                for k in order:
                    if n == 0 and k == order[0]:
                        pe.wait_ge(pairs_act, BATCHES * (t + 1))
                        pe.wait_ge(pairs_dve, BATCHES * (t + 1))
                    if n == 0 and k == 0:
                        wait_emptied(pe, fill_no[("few", t)])
                    last = nc.tensor.matmul(h1_out(t, n), W1P[:, k, n * P:(n + 1) * P], PAIRS[:, k, t * P:(t + 1) * P],
                                            start=False, stop=(k == order[-1]))
                if t == TILES - 1 or n == HC1 - 1:
                    last.then_inc(h1_sum, 1)

            def layer2(t):
                if t:
                    pe.wait_ge(y_ready, t)
                final = t == TILES - 1
                order = [(n, k) for n in range(HC2) for k in range(HC1)]
                if final:
                    order = [(n, k) for k in range(HC1) for n in range(HC2)]
                for n, k in order:
                    if n == 0 and final and k % 2:
                        pe.wait_ge(h1_ready_dve, k // 2 + 1)
                    elif n == 0:
                        pe.wait_ge(h1_ready, HC1 * t + (k // 2 if final else k) + 1)
                    last = nc.tensor.matmul(h2_out(t, n), W2[:, k, n * P:(n + 1) * P],
                                            h1[:, k, :], start=(k == 0), stop=(k == HC1 - 1))
                    if k == HC1 - 1 and (final or n == HC2 - 1):
                        last.then_inc(h2_sum, 1)

            def layer3(t):
                final = t == TILES - 1
                for k in range(HC2):
                    if final and k == 1:
                        pe.wait_ge(h2_ready_dve, 1)
                    elif k == 0:
                        pe.wait_ge(h2_ready, HC2 * t + (1 if final else HC2))
                    last = nc.tensor.matmul(y_out(t), W3[:, k:k + 1], h2[:, k, :],
                                            start=(k == 0), stop=(k == HC2 - 1))
                last.then_inc(y_sum, 1)

            for item in fills[:n_first]:
                fill(item)
            pe.wait_ge(w1_in, 32)
            pe.wait_ge(w2_in, 32)
            pe.wait_ge(padding_clear, 1)
            for t in range(TILES):
                if t:
                    turn_few(t)
                for i in range(BATCHES):
                    gram(t, i)
                    if 0 < t < TILES - 1 and i == 0:
                        layer3(t - 1)
                    if t == 0 and i == FEW_AFTER:
                        turn_few(t)
                if t == TILES - 1:
                    break
                fill(between[t][0])
                if t:
                    pe.wait_ge(h1_ready, HC1 * t)
                for n in range(HC1):
                    layer1_dense(t, n)
                    layer1_pairs(t, n)
                    for item in between[t][n + 1:n + 2]:
                        fill(item)
                for item in late[t][:BEFORE_L2[t]]:
                    fill(item)
                layer2(t)
                for item in late[t][BEFORE_L2[t]:]:
                    if t == TILES - 2 and item is late[t][-1]:
                        layer3(t)
                    fill(item)
            pe.wait_ge(pairs_act, BATCHES * (t + 1) - 1)
            pe.wait_ge(pairs_dve, BATCHES * (t + 1) - 1)
            for n in range(HC1 - 1):
                layer1_dense(t, n)
            for n in range(HC1):
                if n == HC1 - 1:
                    layer1_dense(t, n)
                layer1_pairs(t, n)
            layer2(t)
            layer3(t)


def few_place(i):
    chunk, i = divmod(i, FEW_PER_CHUNK)
    quadrant, row = divmod(i, SPARE)
    return SLOTS * quadrant + NVEC + row, chunk


def pair_rows():
    rows = []
    slot = {f: s for s, f in enumerate(SLOT_FIELD)}
    n = 0
    for i in range(NVEC):
        for j in range(i + 1, NVEC):
            a, g = sorted((slot[i], slot[j]))
            if g < FIRST:
                rows.append((*few_place(FEW.index((a, g))), n))
            else:
                s, k = divmod(g - FIRST, PART_COLS)
                rows.append((32 * s + a, k, n))
            n += 1
    return rows, n


def kernel(**inputs):
    import numpy as _np
    import concourse.bacc as _bacc
    from concourse import mybir as _mybir
    from concourse.bass_utils import run_bass_kernel_spmd as _run

    nc = _bacc.Bacc("TRN2", target_bir_lowering=False, num_devices=1)
    arrays, args = {}, {}

    def give(name, a):
        a = _np.ascontiguousarray(a)
        arrays[f"in_{name}_dram"] = a
        args[name] = nc.dram_tensor(f"in_{name}_dram", a.shape, _mybir.dt.from_np(a.dtype), kind="ExternalInput").ap()
        return args[name]

    x = give("r_dense_x", inputs["r_dense_x"])
    ids = give("ids", inputs["ids"])
    ids_t = give("ids_t", _np.asarray(inputs["ids"]).T)
    chunk_numbers = give("chunk_numbers", _np.repeat(_np.arange(CHUNKS, dtype=_np.float16), BATCH)
                         .reshape(1, CHUNKS, BATCH))
    tables = [give(f"tbl_{f}", inputs[f"tbl_{f}"]) for f in range(NTAB)]
    w1 = _np.asarray(inputs["W_top1"])
    where, n_pairs = pair_rows()
    p, k, r = (_np.array(c) for c in zip(*where))
    w1_pairs = _np.zeros((P, PART_COLS, H1), w1.dtype)
    w1_pairs[p, k] = w1[r]
    w1p = give("w1_pairs", w1_pairs)
    w1d = give("w1_dense", w1[n_pairs:])
    b1 = give("b_top1", inputs["b_top1"])
    w2 = give("W_top2", inputs["W_top2"])
    b2 = give("b_top2", inputs["b_top2"])
    w3 = give("W_top3", inputs["W_top3"])
    out = nc.dram_tensor("out_0_dram", (BATCH, 1), _mybir.dt.float32, kind="ExternalOutput").ap()
    build(nc, x, ids, ids_t, chunk_numbers, tables, w1p, w1d, b1, w2, b2, w3, out)
    r = _run(nc, [arrays], core_ids=[0])
    return r.results[0]["out_0_dram"]
```
